# Optimizing a Trainium2 kernel written in Bass

```python
import numpy as np
import jax
import jax.numpy as jnp

def _softmax(x, axis=-1):
    return jax.nn.softmax(x, axis=axis)

def _gelu(x):
    return jax.nn.gelu(x, approximate=True)

def _silu(x):
    return jax.nn.silu(x)

def _sigmoid(x):
    return jax.nn.sigmoid(x)

def _layernorm(x, axis=-1, eps=1e-05):
    m = jnp.mean(x, axis=axis, keepdims=True)
    v = jnp.var(x, axis=axis, keepdims=True)
    return (x - m) / jnp.sqrt(v + eps)

def _scatter_add(tgt, idx, src, axis=0):
    return tgt.at[idx].add(src)

def _segment_sum(src, seg, n):
    return jax.ops.segment_sum(src, seg, n)
kernel_name = 'mk_adj_preln_d2_adj_r2_0d8f07'

def setup_inputs(seed: int=0):
    np.random.seed(seed)
    _w = jnp.asarray

    def _rec_inputs():
        import jax
        import jax.numpy as jnp
        _gk = jax.random.key(seed)
        x = -0.0002422 + 1 * jax.random.normal(jax.random.fold_in(_gk, 1), (64, 128, 512), jnp.float32)
        _w = (1.0 + jnp.arange(128, dtype=jnp.float32)) ** (-0.5)
        _w = _w / _w.mean()
        _pij = jnp.clip(0.125 * _w[:, None] * _w[None, :], 0.0, 1.0)
        _a = jax.random.uniform(jax.random.fold_in(_gk, 2), (64, 128, 128)) < _pij
        adj = _a.astype(jnp.int32)
        return (x, adj)
    x, adj = _rec_inputs()

    def _L0_gnn_setup():
        import jax, jax.numpy as jnp
        import numpy as np
        IN_DIM = 512
        OUT_DIM = 512
        BATCH = 128
        NUM_OBJS = 100
        key = jax.random.key(seed)
        k1, k2, k3, k4, k5 = jax.random.split(key, 5)
        stdv = 1.0 / np.sqrt(OUT_DIM)
        feature = jax.random.normal(k1, (BATCH, NUM_OBJS, IN_DIM), dtype=jnp.float32)
        graph = jax.random.randint(k2, (BATCH, NUM_OBJS, NUM_OBJS), 0, 2, dtype=jnp.int32)
        weight = jax.random.uniform(k3, (IN_DIM, OUT_DIM), dtype=jnp.float32, minval=-stdv, maxval=stdv)
        wq = jax.random.uniform(k4, (IN_DIM, OUT_DIM), dtype=jnp.float32, minval=-stdv, maxval=stdv)
        wk = jax.random.uniform(k5, (IN_DIM, OUT_DIM), dtype=jnp.float32, minval=-stdv, maxval=stdv)
        return {'feature': feature, 'graph': graph, 'weight': weight, 'wq': wq, 'wk': wk}
    _L0_gnn_all = _L0_gnn_setup()
    _L0_gnn_in = {k: v for k, v in _L0_gnn_all.items() if k in ('weight', 'wq', 'wk')}
    del _L0_gnn_all

    def _L1_gnn_setup():
        import jax, jax.numpy as jnp
        import numpy as np
        import math
        D_MODEL = 512
        N_HEADS = 16
        D_HEAD = D_MODEL // N_HEADS
        B, S = (4, 1024)
        key = jax.random.key(seed)
        ks = jax.random.split(key, 10)
        x = jax.random.normal(ks[0], (B, S, D_MODEL), dtype=jnp.float32)
        mask = jax.random.randint(ks[1], (B, S, S), 0, 2, dtype=jnp.int32)
        eye = jnp.eye(S, dtype=jnp.int32)[None]
        mask = jnp.maximum(mask, eye)
        std = 1.0 / math.sqrt(D_MODEL)
        Wq = jax.random.normal(ks[2], (D_MODEL, D_MODEL), dtype=jnp.float32) * std
        Wk = jax.random.normal(ks[3], (D_MODEL, D_MODEL), dtype=jnp.float32) * std
        Wv = jax.random.normal(ks[4], (D_MODEL, D_MODEL), dtype=jnp.float32) * std
        Wo = jax.random.normal(ks[5], (D_MODEL, D_MODEL), dtype=jnp.float32) * std
        bq = jnp.zeros((D_MODEL,), dtype=jnp.float32)
        bk = jnp.zeros((D_MODEL,), dtype=jnp.float32)
        bv = jnp.zeros((D_MODEL,), dtype=jnp.float32)
        bo = jnp.zeros((D_MODEL,), dtype=jnp.float32)
        return {'x': x, 'mask': mask, 'Wq': Wq, 'bq': bq, 'Wk': Wk, 'bk': bk, 'Wv': Wv, 'bv': bv, 'Wo': Wo, 'bo': bo}
    _L1_gnn_all = _L1_gnn_setup()
    _L1_gnn_in = {k: v for k, v in _L1_gnn_all.items() if k in ('Wq', 'bq', 'Wk', 'bk', 'Wv', 'bv', 'Wo', 'bo')}
    del _L1_gnn_all
    return {'x': x, 'adj': adj, 'L0_gnn_weight': _L0_gnn_in['weight'], 'L0_gnn_wq': _L0_gnn_in['wq'], 'L0_gnn_wk': _L0_gnn_in['wk'], 'L1_gnn_Wq': _L1_gnn_in['Wq'], 'L1_gnn_bq': _L1_gnn_in['bq'], 'L1_gnn_Wk': _L1_gnn_in['Wk'], 'L1_gnn_bk': _L1_gnn_in['bk'], 'L1_gnn_Wv': _L1_gnn_in['Wv'], 'L1_gnn_bv': _L1_gnn_in['bv'], 'L1_gnn_Wo': _L1_gnn_in['Wo'], 'L1_gnn_bo': _L1_gnn_in['bo']}

def reference(x, adj, L0_gnn_weight, L0_gnn_wq, L0_gnn_wk, L1_gnn_Wq, L1_gnn_bq, L1_gnn_Wk, L1_gnn_bk, L1_gnn_Wv, L1_gnn_bv, L1_gnn_Wo, L1_gnn_bo):
    import jax
    import jax.numpy as jnp

    def _L0_gnn_ref(feature, graph, weight, wq, wk):
        import jax, jax.numpy as jnp
        import numpy as np
        IN_DIM = 512
        OUT_DIM = 512
        BATCH = 128
        NUM_OBJS = 100
        output = jnp.einsum('bni,io->bno', feature, weight)
        q = jnp.einsum('bni,io->bno', feature, wq)
        k = jnp.einsum('bni,io->bno', feature, wk)
        alpha = jnp.einsum('bno,bmo->bnm', q, k)
        alpha = jnp.maximum(alpha, 0.0) * (graph != 0).astype(alpha.dtype)
        alpha = jax.nn.softmax(alpha, axis=1)
        return jnp.einsum('bnm,bmo->bno', alpha, output)

    def _L1_gnn_ref(x, mask, Wq, bq, Wk, bk, Wv, bv, Wo, bo):
        import jax, jax.numpy as jnp
        import numpy as np
        import math
        D_MODEL = 512
        N_HEADS = 16
        D_HEAD = D_MODEL // N_HEADS
        B, S = (4, 1024)
        b, s, _ = x.shape
        scale = 1.0 / math.sqrt(D_HEAD)

        def heads(t):
            return t.reshape(b, s, N_HEADS, D_HEAD).transpose(0, 2, 1, 3)
        q = heads(x @ Wq + bq)
        k = heads(x @ Wk + bk)
        v = heads(x @ Wv + bv)
        scores = jnp.einsum('bhqd,bhkd->bhqk', q, k) * scale
        scores = jnp.where(mask[:, None] == 0, -jnp.inf, scores)
        attn = jax.nn.softmax(scores, axis=-1)
        out = jnp.einsum('bhqk,bhkd->bhqd', attn, v)
        out = out.transpose(0, 2, 1, 3).reshape(b, s, D_MODEL)
        return out @ Wo + bo
    h = jnp.maximum(_layernorm(x, axis=-1), 0.0)
    x = x + _L0_gnn_ref(h, adj, L0_gnn_weight, L0_gnn_wq, L0_gnn_wk)
    h = jnp.maximum(_layernorm(x, axis=-1), 0.0)
    x = x + _L1_gnn_ref(h, adj, L1_gnn_Wq, L1_gnn_bq, L1_gnn_Wk, L1_gnn_bk, L1_gnn_Wv, L1_gnn_bv, L1_gnn_Wo, L1_gnn_bo)
    return x

_drawn_inputs = setup_inputs


def setup_inputs(seed=0):
    import zlib

    import numpy as np

    out = dict(_drawn_inputs(seed))
    spreads = {'L1_gnn_bq': (0.0, 0.8),
     'L1_gnn_bk': (0.0, 0.8),
     'L1_gnn_bv': (0.0, 0.1),
     'L1_gnn_bo': (0.0, 0.1)}
    factors = {}
    for name, (base, spread) in spreads.items():
        noise = np.random.default_rng([zlib.crc32(name.encode()), seed]).standard_normal(out[name].shape)
        drawn = base * np.exp(spread * noise) if base else spread * noise
        out[name] = jnp.asarray(drawn.astype(out[name].dtype))
    for name, factor in factors.items():
        out[name] = (out[name] * factor).astype(out[name].dtype)
    return out
```

```python
from contextlib import ExitStack

import concourse.bass as bass
from concourse import mybir

F32 = mybir.dt.float32
F32R = mybir.dt.float32r
I32 = mybir.dt.int32
ALU = mybir.AluOpType
ACT = mybir.ActivationFunctionType
AXIS = mybir.AxisListType

P = 128
D = 512
C = D // P
HEADS = 16
DH = D // HEADS
HC = P // DH
PAIR = 2
UNITS = C * PAIR
SLOTS = 4
SCALE = float(DH) ** -0.5
EPS = 1e-5
BIG = 1e38


def graph_layers_kernel(nc, x, adj, w0, wq0, wk0, wq1, bq1, wk1, bk1, wv1, bv1, wo1, bo1, out):
    graphs = x.shape[0]
    pairs = graphs // PAIR
    x_pairs = x.rearrange("(g b) n d -> g n b d", b=PAIR)
    adj_pairs = adj.rearrange("(g b) n m -> g n b m", b=PAIR)
    out_pairs = out.rearrange("(g b) n d -> g n b d", b=PAIR)

    ctx = ExitStack()
    with ctx:
        def sb(name, shape, dtype=F32):
            return ctx.enter_context(nc.sbuf_tensor(name, shape, dtype))

        def sem(name):
            return ctx.enter_context(nc.semaphore(name))

        def parts(name):
            return sb(name + "_hi", [P, C, D], F32R), sb(name + "_lo", [P, C, D], F32R)

        m_hi, m_lo = parts("m")
        w_hi, w_lo = parts("w")
        q_hi, q_lo = parts("wq")
        k_hi, k_lo = parts("wk")
        v_hi, v_lo = parts("wv")
        o_hi, o_lo = parts("wo")
        bq = sb("bq", [P, C])
        bk = sb("bk", [P, C])
        bv = sb("bv", [P, C])
        bo = sb("bo", [P, D])
        ident = sb("ident", [P, P])
        wT = sb("wT", [P, 2, C, D])

        xs = sb("xs", [P, 2, PAIR, D])
        adj_sb = sb("adj_sb", [P, PAIR, P], I32)
        edge = sb("edge", [P, PAIR, P])
        edgeT = sb("edgeT", [P, PAIR, P])
        has_edge = sb("has_edge", [P, PAIR])
        has_edge_r = sb("has_edge_r", [P, PAIR])
        low = sb("low", [P, PAIR])
        mask_add = sb("mask_add", [P, 2, PAIR, P])
        stats = sb("stats", [P, PAIR, 6])
        mean_var = sb("mean_var", [P, PAIR, 2])
        var_eps = sb("var_eps", [P, PAIR])
        minus_half = sb("minus_half", [P, PAIR])
        rstd = sb("rstd", [P, PAIR])
        xn0 = sb("xn0", [P, PAIR, D])
        xn1 = sb("xn1", [P, PAIR, D])
        hT0 = sb("hT0", [P, C, PAIR, P])
        hT0_hi = sb("hT0_hi", [P, C, PAIR, P], F32R)
        hT0_lo = sb("hT0_lo", [P, C, PAIR, P], F32R)
        hT1_hi = sb("hT1_hi", [P, C, PAIR, P], F32R)
        hT1_lo = sb("hT1_lo", [P, C, PAIR, P], F32R)
        tT = sb("tT", [P, C, PAIR, P])
        alphaT = sb("alphaT", [P, PAIR, P])
        alpha_nmax = sb("alpha_nmax", [P, PAIR])
        alpha_sum = sb("alpha_sum", [P, PAIR])
        alpha_rsum = sb("alpha_rsum", [P, PAIR])
        hw = sb("hw", [P, PAIR, D])
        v = sb("v", [P, PAIR, D])
        qT = sb("qT", [P, PAIR, P])
        kbd = sb("kbd", [P, PAIR, HC, P])
        probs = sb("probs", [P, SLOTS, HC, P])
        nmax = sb("nmax", [P, SLOTS, HC])
        sums = sb("sums", [P, SLOTS, HC])
        rsums = sb("rsums", [P, SLOTS, HC])
        probsT = sb("probsT", [P, SLOTS, HC, P])
        attT_hi = sb("attT_hi", [P, C, PAIR, P], F32R)
        attT_lo = sb("attT_lo", [P, C, PAIR, P], F32R)

        def bank(name):
            return ctx.enter_context(nc.psum_tensor(name, [P, D], F32))

        score_bank = [bank("score0"), bank("score1")]
        tr_bank = bank("tr")
        pv_bank = bank("pv")
        l1_bank = [bank("l1a"), bank("l1b")]
        l0_bank = [bank("l0a"), bank("l0b")]

        wraw_in = [sem(f"wraw_in{i}") for i in range(7)]
        bias_in = sem("bias_in")
        ident_zero = sem("ident_zero")
        ident_ready = sem("ident_ready")
        kbd_zero = sem("kbd_zero")
        wT_done = sem("wT_done")
        wT_ready = sem("wT_ready")
        m_done = sem("m_done")
        m_hi_ready = sem("m_hi_ready")
        m_ready = sem("m_ready")
        split_hi = sem("split_hi")
        split_done = sem("split_done")
        x_in = sem("x_in")
        adj_in = sem("adj_in")
        stored = sem("stored")
        ln_stats = sem("ln_stats")
        stats_seen = sem("stats_seen")
        ln_aggr = sem("ln_aggr")
        ln_var = sem("ln_var")
        ln_rstd = sem("ln_rstd")
        exponent_ready = sem("exponent_ready")
        edge_ready = sem("edge_ready")
        edge_any = sem("edge_any")
        edge_rec = sem("edge_rec")
        low_ready = sem("low_ready")
        mask_ready = sem("mask_ready")
        xn0_ready = sem("xn0_ready")
        t0_done = sem("t0_done")
        hT0_ready = sem("hT0_ready")
        hT0_hi_ready = sem("hT0_hi_ready")
        hT0_split = sem("hT0_split")
        t_done = sem("t_done")
        tT_ready = sem("tT_ready")
        alpha_done = sem("alpha_done")
        edgeT_done = sem("edgeT_done")
        edgeT_ready = sem("edgeT_ready")
        alpha_masked = sem("alpha_masked")
        alpha_max = sem("alpha_max")
        alpha_exp = sem("alpha_exp")
        alpha_ready = sem("alpha_ready")
        hw_done = sem("hw_done")
        hw_ready = sem("hw_ready")
        ao_done = sem("ao_done")
        x1_ready = sem("x1_ready")
        xn1_ready = sem("xn1_ready")
        bo_added = sem("bo_added")
        t1_done = sem("t1_done")
        hT1_hi_ready = sem("hT1_hi_ready")
        hT1_split = sem("hT1_split")
        v_done = sem("v_done")
        v_ready = sem("v_ready")
        qk_done = sem("qk_done")
        qk_ready = sem("qk_ready")
        score_done = sem("score_done")
        score_masked = sem("score_masked")
        max_ready = sem("max_ready")
        exp_ready = sem("exp_ready")
        rsum_ready = sem("rsum_ready")
        probs_ready = sem("probs_ready")
        tr_done = sem("tr_done")
        probsT_ready = sem("probsT_ready")
        pv_done = sem("pv_done")
        att_hi_ready = sem("att_hi_ready")
        att_split = sem("att_split")
        o_done = sem("o_done")
        y_ready = sem("y_ready")

        def wait(eng, semaphore, g, per_pair, more):
            value = g * per_pair + more
            if not isinstance(value, int) or value > 0:
                eng.wait_ge(semaphore, value)

        stage = [probs[:].rearrange("p s h k -> p s (h k)"), probsT[:].rearrange("p s h k -> p s (h k)")]
        raw = [wq0, wk0, w0, wq1, wk1, wv1, wo1]
        split_into = [None, None, (w_hi, w_lo), (q_hi, q_lo), (k_hi, k_lo), (v_hi, v_lo), (o_hi, o_lo)]

        def over_pairs(eng, step):
            step(0, 0, True)
            with eng.Fori(1, pairs - 2, 2) as g:
                step(g, 1, True)
                step(g + 1, 0, True)
            step(pairs - 1, 1, False)

        block = ctx.enter_context(nc.Block())

        @block.sync
        def _(sp):
            sp.dma_start(xs[:, 0], x_pairs[0]).then_inc(x_in, 16)
            sp.dma_start(adj_sb[:], adj_pairs[0]).then_inc(adj_in, 16)
            for i, w in enumerate(raw):
                if i in (2, 3):
                    sp.wait_ge(wT_done, C * (i - 1))
                if i >= 4:
                    sp.wait_ge(split_done, i - 3)
                sp.dma_start(stage[i % 2], w.rearrange("(c p) o -> p c o", p=P)).then_inc(wraw_in[i], 16)

            def step(g, parity, more):
                if more:
                    wait(sp, stored, g, 16, 0)
                    sp.wait_ge(x_in, 16)
                    sp.dma_start(xs[:, 1 - parity], x_pairs[g + 1]).then_inc(x_in, 16)
                    wait(sp, mask_ready, g, 1, 1)
                    sp.wait_ge(x_in, 16)
                    sp.dma_start(adj_sb[:], adj_pairs[g + 1]).then_inc(adj_in, 16)
                wait(sp, y_ready, g, 2, 2)
                sp.dma_start(out_pairs[g], xs[:, parity]).then_inc(stored, 16)

            over_pairs(sp, step)
            sp.wait_ge(stored, 16 * pairs)

        @block.gpsimd
        def _(pool):
            pool.memset(ident[:], 0.0).then_inc(ident_zero, 1)
            pool.memset(kbd[:], 0.0).then_inc(kbd_zero, 1)
            pool.wait_ge(ident_zero, 1)
            pool.affine_select(out=ident[:], in_=ident[:], compare_op=ALU.not_equal, fill=1.0, base=0,
                               pattern=[[-1, P]], channel_multiplier=1).then_inc(ident_ready, 1)
            pool.memset(minus_half[:], -0.5).then_inc(exponent_ready, 1)
            pool.wait_ge(exponent_ready, 1)

            def inverse_root(n, which):
                wait(pool, ln_var, n, 2, which + 1)
                pool.tensor_tensor(rstd[:], var_eps[:], minus_half[:], ALU.pow).then_inc(ln_rstd, 1)

            inverse_root(0, 0)
            inverse_root(0, 1)
            pool.wait_ge(bias_in, 16 * 4)

            def step(g, parity, more):
                wait(pool, xn1_ready, g, 1, 1)
                pool.tensor_tensor(xs[:, parity], xs[:, parity],
                                   bo[:].rearrange("p (a d) -> p a d", a=1).to_broadcast([P, PAIR, D]),
                                   ALU.add).then_inc(bo_added, 1)
                if more:
                    inverse_root(g + 1, 0)
                    inverse_root(g + 1, 1)

            over_pairs(pool, step)

        @block.scalar
        def _(act):
            act.dma_start(bq[:], bq1.rearrange("(c p) -> p c", p=P),
                          allow_slow_non_contiguous=True).then_inc(bias_in, 16)
            act.dma_start(bk[:], bk1.rearrange("(c p) -> p c", p=P),
                          allow_slow_non_contiguous=True).then_inc(bias_in, 16)
            act.dma_start(bv[:], bv1.rearrange("(c p) -> p c", p=P),
                          allow_slow_non_contiguous=True).then_inc(bias_in, 16)
            act.dma_start(bo[:], bo1.rearrange("(a d) -> a d", a=1).to_broadcast([P, D])).then_inc(bias_in, 16)
            for i in range(2 * C):
                act.wait_ge(wT_done, i + 1)
                nc.scalar.activation(wT[:, i // C, i % C], l0_bank[i % 2][:], ACT.Copy).then_inc(wT_ready, 1)
            for r in range(C):
                act.wait_ge(m_done, r + 1)
                nc.scalar.activation(m_hi[:, r], l1_bank[r % 2][:], ACT.Copy).then_inc(m_hi_ready, 1)

            def relu_h0(n):
                for k in range(2):
                    wait(act, t0_done, n, 2, k + 1)
                    nc.scalar.activation(hT0[:, 2 * k:2 * k + 2].rearrange("p c b n -> p (c b n)"),
                                         l0_bank[k][:], ACT.Relu).then_inc(hT0_ready, 1)

            def copy_t(n, k):
                wait(act, t_done, n, 2, k + 1)
                nc.scalar.activation(tT[:, 2 * k:2 * k + 2].rearrange("p c b n -> p (c b n)"),
                                     l0_bank[k][:], ACT.Copy).then_inc(tT_ready, 1)

            def exp_alpha(n):
                wait(act, alpha_max, n, 1, 1)
                for b in range(PAIR):
                    last = nc.scalar.activation(alphaT[:, b], alphaT[:, b], ACT.Exp,
                                                bias=alpha_nmax[:, b:b + 1],
                                                accum_out=alpha_sum[:, b:b + 1])
                last.then_inc(alpha_exp, 1)

            def scale_hw(n, b):
                wait(act, alpha_ready, n, 1, 1)
                wait(act, hw_done, n, 2, b + 1)
                nc.scalar.activation(hw[:, b], l0_bank[b][:], ACT.Copy,
                                     scale=alpha_rsum[:, b:b + 1]).then_inc(hw_ready, 1)

            def relu_h1(n):
                for k in range(2):
                    wait(act, t1_done, n, 2, k + 1)
                    nc.scalar.activation(hT1_hi[:, 2 * k:2 * k + 2].rearrange("p c b n -> p (c b n)"),
                                         l0_bank[k][:], ACT.Relu).then_inc(hT1_hi_ready, 1)

            def copy_v(g, b):
                wait(act, v_done, g, 2, b + 1)
                nc.scalar.activation(v[:, b], l1_bank[1 - b][:], ACT.Copy).then_inc(v_ready, 1)

            def place_qk(g, c):
                wait(act, qk_done, g, 4, c + 1)
                bank_qk = l1_bank[c % 2]
                nc.scalar.activation(qT[:].rearrange("p b n -> p (b n)"), bank_qk[:, 0:PAIR * P],
                                     ACT.Identity, bias=bq[:, c:c + 1])
                for j in range(HC):
                    rows = slice(DH * j, DH * j + DH)
                    last = nc.scalar.activation(
                        kbd[rows, :, j], bank_qk[rows, PAIR * P:].rearrange("p (b n) -> p b n", b=PAIR),
                        ACT.Identity, bias=bk[rows, c:c + 1])
                last.then_inc(qk_ready, 1)

            def exp_scores(g, u):
                s = u % SLOTS
                wait(act, max_ready, g, UNITS, u + 1)
                for j in range(HC):
                    last = nc.scalar.activation(probs[:, s, j], probs[:, s, j], ACT.Exp,
                                                bias=nmax[:, s, j:j + 1], accum_out=sums[:, s, j:j + 1])
                last.then_inc(exp_ready, 1)

            def copy_probsT(g, u):
                wait(act, tr_done, g, UNITS, u + 1)
                nc.scalar.activation(probsT[:, u % SLOTS].rearrange("p h q -> p (h q)"), tr_bank[:],
                                     ACT.Copy).then_inc(probsT_ready, 1)

            def att_hi(g, c):
                wait(act, pv_done, g, C, c + 1)
                nc.scalar.activation(attT_hi[:, c].rearrange("p b n -> p (b n)"), pv_bank[:, 0:PAIR * P],
                                     ACT.Identity, bias=bv[:, c:c + 1]).then_inc(att_hi_ready, 1)

            relu_h0(0)
            copy_t(0, 0)
            copy_t(0, 1)
            exp_alpha(0)
            scale_hw(0, 0)
            scale_hw(0, 1)
            relu_h1(0)
            act.wait_ge(bias_in, 16 * 4)
            act.wait_ge(kbd_zero, 1)
            act.wait_ge(split_done, 5)

            def step(g, parity, more):
                n = g + 1
                place_qk(g, 0)
                copy_v(g, 0)
                exp_scores(g, 0)
                exp_scores(g, 1)
                copy_v(g, 1)
                place_qk(g, 1)
                copy_probsT(g, 0)
                if more:
                    relu_h0(n)
                copy_probsT(g, 1)
                att_hi(g, 0)
                exp_scores(g, 2)
                exp_scores(g, 3)
                place_qk(g, 2)
                if more:
                    copy_t(n, 0)
                copy_probsT(g, 2)
                copy_probsT(g, 3)
                if more:
                    copy_t(n, 1)
                att_hi(g, 1)
                exp_scores(g, 4)
                exp_scores(g, 5)
                place_qk(g, 3)
                copy_probsT(g, 4)
                if more:
                    exp_alpha(n)
                exp_scores(g, 6)
                if more:
                    scale_hw(n, 0)
                copy_probsT(g, 5)
                att_hi(g, 2)
                exp_scores(g, 7)
                if more:
                    scale_hw(n, 1)
                copy_probsT(g, 6)
                copy_probsT(g, 7)
                att_hi(g, 3)
                if more:
                    relu_h1(n)

            over_pairs(act, step)

        @block.vector
        def _(dve):
            def norm_stats(which, n, parity):
                for b in range(PAIR):
                    if which == 1:
                        wait(dve, x1_ready, n, 2, b + 1)
                    nc.vector.bn_stats(stats[:, b], xs[:, parity, b]).then_inc(ln_stats, 1)
                wait(dve, ln_stats, n, 4, 2 * which + 2)
                dve.sem_inc(stats_seen, 1)
                for b in range(PAIR):
                    nc.vector.bn_aggr(mean_var[:, b], stats[:, b]).then_inc(ln_aggr, 1)
                wait(dve, ln_aggr, n, 4, 2 * which + 2)
                nc.vector.tensor_scalar(var_eps[:].rearrange("p (b a) -> p b a", a=1), mean_var[:, :, 1:2], EPS,
                                        None, ALU.add).then_inc(ln_var, 1)

            def norm_apply(which, n, parity, xn):
                wait(dve, ln_rstd, n, 2, which + 1)
                for b in range(PAIR):
                    last = nc.vector.tensor_scalar(xn[:, b], xs[:, parity, b], mean_var[:, b, 0:1],
                                                   rstd[:, b:b + 1], ALU.subtract, ALU.mult)
                last.then_inc([xn0_ready, xn1_ready][which], 1)

            def norm0_stats(n, parity):
                wait(dve, x_in, n, 16, 16)
                norm_stats(0, n, parity)

            def masks(n, parity):
                wait(dve, adj_in, n, 16, 16)
                nc.vector.tensor_scalar(edge[:], adj_sb[:], 0.0, None, ALU.not_equal).then_inc(edge_ready, 1)
                wait(dve, edge_ready, n, 1, 1)
                nc.vector.tensor_reduce(has_edge[:], edge[:], AXIS.X, ALU.max).then_inc(edge_any, 1)
                wait(dve, edge_any, n, 1, 1)
                nc.vector.reciprocal(has_edge_r[:], has_edge[:]).then_inc(edge_rec, 1)
                wait(dve, edge_rec, n, 1, 1)
                nc.vector.scalar_tensor_tensor(low[:], has_edge_r[:], -BIG, has_edge[:], ALU.mult,
                                               ALU.mult).then_inc(low_ready, 1)
                wait(dve, low_ready, n, 1, 1)
                for b in range(PAIR):
                    last = nc.vector.tensor_scalar(mask_add[:, parity, b], adj_sb[:, b], 0.0, low[:, b:b + 1],
                                                   ALU.is_equal, ALU.mult)
                last.then_inc(mask_ready, 1)

            def split_h0(n):
                wait(dve, hT0_ready, n, 2, 2)
                nc.vector.tensor_copy(hT0_hi[:], hT0[:]).then_inc(hT0_hi_ready, 1)
                wait(dve, hT0_hi_ready, n, 1, 1)
                nc.vector.tensor_tensor(hT0_lo[:], hT0[:], hT0_hi[:].bitcast(F32),
                                        ALU.subtract).then_inc(hT0_split, 1)

            def mask_alpha(n):
                wait(dve, edgeT_done, n, 1, 1)
                nc.vector.tensor_copy(edgeT[:].rearrange("p b n -> p (b n)"),
                                      l0_bank[1][:, 0:PAIR * P]).then_inc(edgeT_ready, 1)
                wait(dve, edgeT_ready, n, 1, 1)
                wait(dve, alpha_done, n, 1, 1)
                nc.vector.scalar_tensor_tensor(alphaT[:].rearrange("p b n -> p (b n)"),
                                               l0_bank[0][:, 0:PAIR * P], 0.0,
                                               edgeT[:].rearrange("p b n -> p (b n)"),
                                               ALU.max, ALU.mult).then_inc(alpha_masked, 1)
                wait(dve, alpha_masked, n, 1, 1)
                nc.vector.tensor_reduce(alpha_nmax[:], alphaT[:], AXIS.X, ALU.max,
                                        negate=True).then_inc(alpha_max, 1)

            def alpha_sums(n):
                wait(dve, alpha_exp, n, 1, 1)
                nc.vector.reciprocal(alpha_rsum[:], alpha_sum[:]).then_inc(alpha_ready, 1)

            def residual0(n, parity, b):
                wait(dve, ao_done, n, 2, b + 1)
                nc.vector.tensor_tensor(xs[:, parity, b], xs[:, parity, b], l0_bank[b][:],
                                        ALU.add).then_inc(x1_ready, 1)

            def lo_h1(n, k):
                wait(dve, hT1_hi_ready, n, 2, k + 1)
                nc.vector.scalar_tensor_tensor(
                    hT1_lo[:, 2 * k:2 * k + 2].rearrange("p c b n -> p (c b n)"), l0_bank[k][:], 0.0,
                    hT1_hi[:, 2 * k:2 * k + 2].rearrange("p c b n -> p (c b n)").bitcast(F32),
                    ALU.max, ALU.subtract).then_inc(hT1_split, 1)

            def mask_scores(g, parity, u):
                s, b = u % SLOTS, u % PAIR
                wait(dve, score_done, g, UNITS, u + 1)
                wait(dve, tr_done, g, UNITS, u + 1 - SLOTS)
                mask_b = mask_add[:, parity, b:b + 1].to_broadcast([P, HC, P])
                nc.vector.scalar_tensor_tensor(probs[:, s], score_bank[u % 2][:].rearrange("p (h k) -> p h k", h=HC),
                                               SCALE, mask_b, ALU.mult, ALU.add).then_inc(score_masked, 1)
                wait(dve, score_masked, g, UNITS, u + 1)
                nc.vector.tensor_reduce(nmax[:, s], probs[:, s], AXIS.X, ALU.max,
                                        negate=True).then_inc(max_ready, 1)

            def normalise(g, u):
                s = u % SLOTS
                wait(dve, exp_ready, g, UNITS, u + 1)
                nc.vector.reciprocal(rsums[:, s], sums[:, s]).then_inc(rsum_ready, 1)
                wait(dve, rsum_ready, g, UNITS, u + 1)
                nc.vector.tensor_tensor(probs[:, s], probs[:, s],
                                        rsums[:, s].rearrange("p (h a) -> p h a", a=1).to_broadcast([P, HC, P]),
                                        ALU.mult).then_inc(probs_ready, 1)

            def att_lo(g, c):
                wait(dve, att_hi_ready, g, C, c + 1)
                nc.vector.scalar_tensor_tensor(attT_lo[:, c].rearrange("p b n -> p (b n)"),
                                               pv_bank[:, 0:PAIR * P], bv[:, c:c + 1],
                                               attT_hi[:, c].rearrange("p b n -> p (b n)").bitcast(F32),
                                               ALU.add, ALU.subtract).then_inc(att_split, 1)

            def residual1(g, parity, b):
                wait(dve, bo_added, g, 1, 1)
                wait(dve, o_done, g, 2, b + 1)
                nc.vector.tensor_tensor(xs[:, parity, b], xs[:, parity, b], l1_bank[b][:],
                                        ALU.add).then_inc(y_ready, 1)

            def split_weight(i):
                hi, lo = split_into[i]
                dve.wait_ge(wraw_in[i], 16)
                nc.vector.tensor_copy(hi[:], stage[i % 2]).then_inc(split_hi, 1)
                dve.wait_ge(split_hi, i - 1)
                nc.vector.tensor_tensor(lo[:], stage[i % 2], hi[:].bitcast(F32),
                                        ALU.subtract).then_inc(split_done, 1)

            norm0_stats(0, 0)
            masks(0, 0)
            norm_apply(0, 0, 0, xn0)
            for r in range(C):
                dve.wait_ge(m_hi_ready, r + 1)
                nc.vector.tensor_tensor(m_lo[:, r], l1_bank[r % 2][:], m_hi[:, r].bitcast(F32),
                                        ALU.subtract).then_inc(m_ready, 1)
            split_h0(0)
            split_weight(2)
            mask_alpha(0)
            split_weight(3)
            alpha_sums(0)
            split_weight(4)
            residual0(0, 0, 0)
            residual0(0, 0, 1)
            norm_stats(1, 0, 0)
            norm_apply(1, 0, 0, xn1)
            lo_h1(0, 0)
            lo_h1(0, 1)
            split_weight(5)
            split_weight(6)
            dve.wait_ge(bias_in, 16 * 4)

            def step(g, parity, more):
                n = g + 1
                mask_scores(g, parity, 0)
                mask_scores(g, parity, 1)
                if more:
                    norm0_stats(n, 1 - parity)
                normalise(g, 0)
                if more:
                    norm_apply(0, n, 1 - parity, xn0)
                normalise(g, 1)
                if more:
                    split_h0(n)
                mask_scores(g, parity, 2)
                att_lo(g, 0)
                mask_scores(g, parity, 3)
                if more:
                    masks(n, 1 - parity)
                normalise(g, 2)
                normalise(g, 3)
                att_lo(g, 1)
                mask_scores(g, parity, 4)
                mask_scores(g, parity, 5)
                normalise(g, 4)
                normalise(g, 5)
                if more:
                    mask_alpha(n)
                mask_scores(g, parity, 6)
                if more:
                    alpha_sums(n)
                att_lo(g, 2)
                mask_scores(g, parity, 7)
                normalise(g, 6)
                if more:
                    residual0(n, 1 - parity, 0)
                normalise(g, 7)
                if more:
                    residual0(n, 1 - parity, 1)
                    norm_stats(1, n, 1 - parity)
                    norm_apply(1, n, 1 - parity, xn1)
                att_lo(g, 3)
                if more:
                    lo_h1(n, 0)
                residual1(g, parity, 0)
                if more:
                    lo_h1(n, 1)
                residual1(g, parity, 1)

            over_pairs(dve, step)

        @block.tensor
        def _(pe):
            def by_rows(bank_out, hi, lo, b, weight_hi, weight_lo, first=0, end=C):
                for c in range(first, end):
                    nc.tensor.matmul(bank_out[:], hi[:, c, b], weight_hi[:, c], start=(c == 0), stop=False)
                    nc.tensor.matmul(bank_out[:], hi[:, c, b], weight_lo[:, c], start=False, stop=False)
                    last = nc.tensor.matmul(bank_out[:], lo[:, c, b], weight_hi[:, c], start=False,
                                            stop=(c == C - 1))
                return last

            def by_columns(region, weight_hi, weight_lo, cols, hi, lo, before=None):
                for c in range(C):
                    if before is not None:
                        before(c)
                    h_hi = hi[:, c].rearrange("p b n -> p (b n)")
                    h_lo = lo[:, c].rearrange("p b n -> p (b n)")
                    nc.tensor.matmul(region, weight_hi[:, c, cols], h_hi, start=(c == 0), stop=False)
                    nc.tensor.matmul(region, weight_hi[:, c, cols], h_lo, start=False, stop=False)
                    last = nc.tensor.matmul(region, weight_lo[:, c, cols], h_hi, start=False,
                                            stop=(c == C - 1))
                return last

            def chunk(c):
                return slice(c * P, c * P + P)

            def transpose_x(xn, done):
                for k in range(2):
                    for i in range(2 * PAIR):
                        last = nc.tensor.transpose(l0_bank[k][:, chunk(i)], xn[:, i % PAIR, chunk(2 * k + i // PAIR)],
                                                   ident[:])
                    last.then_inc(done, 1)

            def transpose_x0(n):
                wait(pe, xn0_ready, n, 1, 1)
                wait(pe, hT1_split, n, 2, 0)
                transpose_x(xn0, t0_done)

            def project_t(n, c):
                wait(pe, hT0_split, n, 1, 1)
                half = c % 2
                last = by_columns(l0_bank[c // 2][:, half * PAIR * P:(half + 1) * PAIR * P], m_hi, m_lo,
                                  chunk(c), hT0_hi, hT0_lo)
                if half == 1:
                    last.then_inc(t_done, 1)

            def alpha_product(n):
                wait(pe, tT_ready, n, 2, 2)
                for b in range(PAIR):
                    for c in range(C):
                        last = nc.tensor.matmul(l0_bank[0][:, chunk(b)], hT0[:, c, b], tT[:, c, b],
                                                start=(c == 0), stop=(c == C - 1))
                last.then_inc(alpha_done, 1)
                wait(pe, mask_ready, n, 1, 1)
                for b in range(PAIR):
                    last = nc.tensor.transpose(l0_bank[1][:, chunk(b)], edge[:, b], ident[:])
                last.then_inc(edgeT_done, 1)

            def project_hw(n, b):
                wait(pe, alpha_masked, n, 1, 1)
                by_rows(l0_bank[b], hT0_hi, hT0_lo, b, w_hi, w_lo).then_inc(hw_done, 1)

            def alpha_hw(n, b):
                wait(pe, hw_ready, n, 2, b + 1)
                nc.tensor.matmul(l0_bank[b][:], alphaT[:, b], hw[:, b], start=True, stop=True).then_inc(ao_done, 1)

            def transpose_x1(n):
                wait(pe, xn1_ready, n, 1, 1)
                transpose_x(xn1, t1_done)

            def project_qk(g, c):
                def input_split(i):
                    if c == 0 and i % 2 == 0:
                        wait(pe, hT1_split, g, 2, i // 2 + 1)

                if c == 0:
                    wait(pe, y_ready, g, 2, -1)
                if c == 1:
                    wait(pe, v_ready, g, 2, 1)
                if c == 2:
                    wait(pe, v_ready, g, 2, 2)
                if c == 3:
                    wait(pe, qk_ready, g, 4, 2)
                region = l1_bank[c % 2]
                by_columns(region[:, 0:PAIR * P], q_hi, q_lo, chunk(c), hT1_hi, hT1_lo, input_split)
                by_columns(region[:, PAIR * P:], k_hi, k_lo, chunk(c), hT1_hi, hT1_lo).then_inc(qk_done, 1)

            def project_v(g, b):
                if b == 0:
                    wait(pe, y_ready, g, 2, 0)
                else:
                    wait(pe, qk_ready, g, 4, 1)
                by_rows(l1_bank[1 - b], hT1_hi, hT1_lo, b, v_hi, v_lo).then_inc(v_done, 1)

            def scores(g, u):
                c, b = u // PAIR, u % PAIR
                wait(pe, qk_ready, g, 4, c + 1)
                wait(pe, score_masked, g, UNITS, u - 1)
                nc.tensor.matmul(score_bank[u % 2][:], qT[:, b], kbd[:, b].rearrange("p h k -> p (h k)"),
                                 start=True, stop=True).then_inc(score_done, 1)

            def transpose_probs(g, u):
                wait(pe, probs_ready, g, UNITS, u + 1)
                wait(pe, probsT_ready, g, UNITS, u)
                for j in range(HC):
                    last = nc.tensor.transpose(tr_bank[:, chunk(j)], probs[:, u % SLOTS, j], ident[:])
                last.then_inc(tr_done, 1)

            def probs_v(g, u):
                c, b = u // PAIR, u % PAIR
                wait(pe, probsT_ready, g, UNITS, u + 1)
                if b == 0:
                    wait(pe, v_ready, g, 2, 2)
                    wait(pe, att_split, g, C, c)
                for j in range(HC):
                    head = c * HC + j
                    last = nc.tensor.matmul(pv_bank[DH * j:DH * (j + 1), chunk(b)],
                                            v[:, b, head * DH:(head + 1) * DH], probsT[:, u % SLOTS, j],
                                            start=True, stop=True)
                if b == PAIR - 1:
                    last.then_inc(pv_done, 1)

            def project_o(g, b, first, end):
                wait(pe, att_split, g, C, end)
                if first == 0:
                    wait(pe, qk_ready, g, 4, 3 + b)
                last = by_rows(l1_bank[b], attT_hi, attT_lo, b, o_hi, o_lo, first, end)
                if end == C:
                    last.then_inc(o_done, 1)

            pe.wait_ge(ident_ready, 1)
            for i in range(2 * C):
                if i % C == 0:
                    pe.wait_ge(wraw_in[i // C], 16)
                if i >= 2:
                    pe.wait_ge(wT_ready, i - 1)
                for c in range(C):
                    last = nc.tensor.transpose(l0_bank[i % 2][:, chunk(c)], stage[i // C][:, c, chunk(i % C)], ident[:])
                last.then_inc(wT_done, 1)
            pe.wait_ge(wT_ready, 2 * C)
            for r in range(C):
                if r >= 2:
                    pe.wait_ge(m_ready, r - 1)
                for c in range(C):
                    last = nc.tensor.matmul(l1_bank[r % 2][:], wT[:, 0, c, chunk(r)], wT[:, 1, c],
                                            start=(c == 0), stop=(c == C - 1))
                last.then_inc(m_done, 1)
            transpose_x0(0)
            pe.wait_ge(m_ready, C)
            for c in range(C):
                project_t(0, c)
            alpha_product(0)
            pe.wait_ge(split_done, 1)
            project_hw(0, 0)
            project_hw(0, 1)
            alpha_hw(0, 0)
            alpha_hw(0, 1)
            transpose_x1(0)
            pe.wait_ge(split_done, 5)

            def step(g, parity, more):
                n = g + 1
                project_qk(g, 0)
                project_v(g, 0)
                scores(g, 0)
                scores(g, 1)
                project_v(g, 1)
                project_qk(g, 1)
                transpose_probs(g, 0)
                if more:
                    transpose_x0(n)
                probs_v(g, 0)
                transpose_probs(g, 1)
                scores(g, 2)
                probs_v(g, 1)
                scores(g, 3)
                project_qk(g, 2)
                if more:
                    project_t(n, 0)
                    project_t(n, 1)
                transpose_probs(g, 2)
                if more:
                    project_t(n, 2)
                probs_v(g, 2)
                transpose_probs(g, 3)
                if more:
                    project_t(n, 3)
                probs_v(g, 3)
                scores(g, 4)
                scores(g, 5)
                project_qk(g, 3)
                if more:
                    alpha_product(n)
                transpose_probs(g, 4)
                scores(g, 6)
                probs_v(g, 4)
                if more:
                    project_hw(n, 0)
                transpose_probs(g, 5)
                scores(g, 7)
                probs_v(g, 5)
                if more:
                    project_hw(n, 1)
                    alpha_hw(n, 0)
                transpose_probs(g, 6)
                if more:
                    alpha_hw(n, 1)
                probs_v(g, 6)
                transpose_probs(g, 7)
                project_o(g, 0, 0, C - 1)
                probs_v(g, 7)
                project_o(g, 1, 0, C - 1)
                if more:
                    transpose_x1(n)
                project_o(g, 0, C - 1, C)
                project_o(g, 1, C - 1, C)

            over_pairs(pe, step)


_INS = ["x", "adj", "L0_gnn_weight", "L0_gnn_wq", "L0_gnn_wk", "L1_gnn_Wq", "L1_gnn_bq", "L1_gnn_Wk",
        "L1_gnn_bk", "L1_gnn_Wv", "L1_gnn_bv", "L1_gnn_Wo", "L1_gnn_bo"]


def kernel(**inputs):
    import numpy as np
    import concourse.bacc as bacc
    from concourse.bass_utils import run_bass_kernel_spmd

    nc = bacc.Bacc("TRN2", target_bir_lowering=False, num_devices=1)
    arrays, args = {}, []
    for name in _INS:
        a = np.ascontiguousarray(inputs[name])
        arrays[f"in_{name}"] = a
        args.append(nc.dram_tensor(f"in_{name}", a.shape, mybir.dt.from_np(a.dtype), kind="ExternalInput").ap())
    out = nc.dram_tensor("out_x", arrays["in_x"].shape, F32, kind="ExternalOutput").ap()
    graph_layers_kernel(nc, *args, out)
    result = run_bass_kernel_spmd(nc, [arrays], core_ids=[0])
    return result.results[0]["out_x"]
```

```python
from contextlib import ExitStack

import concourse.bass as bass
from concourse import mybir

F32 = mybir.dt.float32
F32R = mybir.dt.float32r
I32 = mybir.dt.int32
ALU = mybir.AluOpType
ACT = mybir.ActivationFunctionType
AXIS = mybir.AxisListType

P = 128
D = 512
C = D // P
HEADS = 16
DH = D // HEADS
HC = P // DH
PAIR = 2
UNITS = C * PAIR
SLOTS = 4
SCALE = float(DH) ** -0.5
EPS = 1e-5
BIG = 1e38


def graph_layers_kernel(nc, x, adj, w0, wq0, wk0, wq1, bq1, wk1, bk1, wv1, bv1, wo1, bo1, out):
    graphs = x.shape[0]
    pairs = graphs // PAIR
    x_pairs = x.rearrange("(g b) n d -> g n b d", b=PAIR)
    adj_pairs = adj.rearrange("(g b) n m -> g n b m", b=PAIR)
    out_pairs = out.rearrange("(g b) n d -> g n b d", b=PAIR)

    ctx = ExitStack()
    with ctx:
        def sb(name, shape, dtype=F32):
            return ctx.enter_context(nc.sbuf_tensor(name, shape, dtype))

        def sem(name):
            return ctx.enter_context(nc.semaphore(name))

        def parts(name):
            return sb(name + "_hi", [P, C, D], F32R), sb(name + "_lo", [P, C, D], F32R)

        m_hi, m_lo = parts("m")
        w_hi, w_lo = parts("w")
        q_hi, q_lo = parts("wq")
        k_hi, k_lo = parts("wk")
        v_hi, v_lo = parts("wv")
        o_hi, o_lo = parts("wo")
        bq = sb("bq", [P, C])
        bk = sb("bk", [P, C])
        bv = sb("bv", [P, C])
        bo = sb("bo", [P, D])
        ident = sb("ident", [P, P])

        x_in_sb = sb("x_in_sb", [P, PAIR, D])
        xs = sb("xs", [P, 2, PAIR, D])
        adj_sb = sb("adj_sb", [P, PAIR, P], I32)
        edge = sb("edge", [P, PAIR, P])
        edgeT = sb("edgeT", [P, PAIR, P])
        has_edge = sb("has_edge", [P, PAIR])
        has_edge_r = sb("has_edge_r", [P, PAIR])
        low = sb("low", [P, PAIR])
        mask_add = sb("mask_add", [P, 2, PAIR, P])
        stats = sb("stats", [P, PAIR, 6])
        mean_var = sb("mean_var", [P, PAIR, 2])
        var_eps = sb("var_eps", [P, PAIR])
        minus_half = sb("minus_half", [P, PAIR])
        rstd = sb("rstd", [P, PAIR])
        xn0 = sb("xn0", [P, PAIR, D])
        xn1 = sb("xn1", [P, PAIR, D])
        hT0 = sb("hT0", [P, C, PAIR, P])
        hT0_hi = sb("hT0_hi", [P, C, PAIR, P], F32R)
        hT0_lo = sb("hT0_lo", [P, C, PAIR, P], F32R)
        hT1_hi = sb("hT1_hi", [P, C, PAIR, P], F32R)
        hT1_lo = sb("hT1_lo", [P, C, PAIR, P], F32R)
        tT = sb("tT", [P, C, PAIR, P])
        alphaT = sb("alphaT", [P, PAIR, P])
        alpha_nmax = sb("alpha_nmax", [P, PAIR])
        alpha_sum = sb("alpha_sum", [P, PAIR])
        alpha_rsum = sb("alpha_rsum", [P, PAIR])
        hw = sb("hw", [P, PAIR, D])
        v = sb("v", [P, PAIR, D])
        qT = sb("qT", [P, PAIR, P])
        kT = sb("kT", [P, PAIR, P])
        qT_hi = sb("qT_hi", [P, 2, PAIR, P], F32R)
        qT_lo = sb("qT_lo", [P, 2, PAIR, P], F32R)
        kbd_hi = sb("kbd_hi", [P, 2, PAIR, HC, P], F32R)
        kbd_lo = sb("kbd_lo", [P, 2, PAIR, HC, P], F32R)
        probs = sb("probs", [P, SLOTS, HC, P])
        nmax = sb("nmax", [P, SLOTS, HC])
        sums = sb("sums", [P, SLOTS, HC])
        rsums = sb("rsums", [P, SLOTS, HC])
        probsT = sb("probsT", [P, SLOTS, HC, P])
        attT_hi = sb("attT_hi", [P, C, PAIR, P], F32R)
        attT_lo = sb("attT_lo", [P, C, PAIR, P], F32R)

        def bank(name):
            return ctx.enter_context(nc.psum_tensor(name, [P, D], F32))

        score_bank = [bank("score0"), bank("score1")]
        tr_bank = bank("tr")
        pv_bank = bank("pv")
        l1_bank = [bank("l1a"), bank("l1b")]
        l0_bank = [bank("l0a"), bank("l0b")]

        wraw_in = [sem(f"wraw_in{i}") for i in range(7)]
        bias_in = sem("bias_in")
        ident_zero = sem("ident_zero")
        ident_ready = sem("ident_ready")
        kbd_zero = sem("kbd_zero")
        wT_done = sem("wT_done")
        wT_ready = sem("wT_ready")
        m_done = sem("m_done")
        m_hi_ready = sem("m_hi_ready")
        m_ready = sem("m_ready")
        split_hi = sem("split_hi")
        split_done = sem("split_done")
        x_in = sem("x_in")
        adj_in = sem("adj_in")
        stored = sem("stored")
        ln_stats = sem("ln_stats")
        stats_seen = sem("stats_seen")
        ln_aggr = sem("ln_aggr")
        ln_var = sem("ln_var")
        ln_rstd = sem("ln_rstd")
        exponent_ready = sem("exponent_ready")
        edge_ready = sem("edge_ready")
        edge_any = sem("edge_any")
        edge_rec = sem("edge_rec")
        low_ready = sem("low_ready")
        mask_ready = sem("mask_ready")
        xn0_ready = sem("xn0_ready")
        t0_done = sem("t0_done")
        hT0_ready = sem("hT0_ready")
        hT0_hi_ready = sem("hT0_hi_ready")
        hT0_split = sem("hT0_split")
        t_done = sem("t_done")
        tT_ready = sem("tT_ready")
        alpha_done = sem("alpha_done")
        edgeT_done = sem("edgeT_done")
        edgeT_ready = sem("edgeT_ready")
        alpha_masked = sem("alpha_masked")
        alpha_max = sem("alpha_max")
        alpha_exp = sem("alpha_exp")
        alpha_ready = sem("alpha_ready")
        hw_done = sem("hw_done")
        hw_ready = sem("hw_ready")
        ao_done = sem("ao_done")
        x1_ready = sem("x1_ready")
        xn1_ready = sem("xn1_ready")
        bo_added = sem("bo_added")
        t1_done = sem("t1_done")
        hT1_hi_ready = sem("hT1_hi_ready")
        hT1_split = sem("hT1_split")
        v_done = sem("v_done")
        v_ready = sem("v_ready")
        qk_done = sem("qk_done")
        qk_ready = sem("qk_ready")
        q_hi_ready = sem("q_hi_ready")
        kbd_hi_ready = sem("kbd_hi_ready")
        qk_split = sem("qk_split")
        score_done = sem("score_done")
        score_masked = sem("score_masked")
        max_ready = sem("max_ready")
        exp_ready = sem("exp_ready")
        rsum_ready = sem("rsum_ready")
        probs_ready = sem("probs_ready")
        tr_done = sem("tr_done")
        probsT_ready = sem("probsT_ready")
        pv_done = sem("pv_done")
        att_hi_ready = sem("att_hi_ready")
        att_split = sem("att_split")
        o_done = sem("o_done")
        y_ready = sem("y_ready")

        def wait(eng, semaphore, g, per_pair, more):
            value = g * per_pair + more
            if not isinstance(value, int) or value > 0:
                eng.wait_ge(semaphore, value)

        wT = [[xn1[:, 0], xn1[:, 1], v[:, 0], v[:, 1]],
              [hw[:, 0], hw[:, 1]] + [tT[:, 2 * k:2 * k + 2].rearrange("p c b n -> p (c b n)") for k in range(2)]]

        stage = [probs[:].rearrange("p s h k -> p s (h k)"), probsT[:].rearrange("p s h k -> p s (h k)")]
        raw = [wq0, wk0, w0, wq1, wk1, wv1, wo1]
        split_into = [None, None, (w_hi, w_lo), (q_hi, q_lo), (k_hi, k_lo), (v_hi, v_lo), (o_hi, o_lo)]

        def over_pairs(eng, step):
            step(0, 0, True)
            with eng.Fori(1, pairs - 2, 2) as g:
                step(g, 1, True)
                step(g + 1, 0, True)
            step(pairs - 1, 1, False)

        block = ctx.enter_context(nc.Block())

        @block.sync
        def _(sp):
            for i, w in enumerate(raw):
                if i == 2:
                    sp.dma_start(x_in_sb[:], x_pairs[0]).then_inc(x_in, 16)
                    sp.dma_start(adj_sb[:], adj_pairs[0]).then_inc(adj_in, 16)
                if i in (2, 3):
                    sp.wait_ge(wT_done, C * (i - 1))
                if i >= 4:
                    sp.wait_ge(split_done, i - 3)
                sp.dma_start(stage[i % 2], w.rearrange("(c p) o -> p c o", p=P)).then_inc(wraw_in[i], 16)

            def step(g, parity, more):
                if more:
                    wait(sp, x1_ready, g, 2, 2)
                    sp.wait_ge(x_in, 16)
                    sp.dma_start(x_in_sb[:], x_pairs[g + 1]).then_inc(x_in, 16)
                    wait(sp, mask_ready, g, 1, 1)
                    sp.wait_ge(x_in, 16)
                    sp.dma_start(adj_sb[:], adj_pairs[g + 1]).then_inc(adj_in, 16)

            over_pairs(sp, step)
            sp.wait_ge(stored, 16 * pairs)

        @block.gpsimd
        def _(pool):
            pool.memset(ident[:], 0.0).then_inc(ident_zero, 1)
            pool.memset(kbd_hi[:].bitcast(F32), 0.0).then_inc(kbd_zero, 1)
            pool.memset(kbd_lo[:].bitcast(F32), 0.0).then_inc(kbd_zero, 1)
            pool.wait_ge(ident_zero, 1)
            pool.affine_select(out=ident[:], in_=ident[:], compare_op=ALU.not_equal, fill=1.0, base=0,
                               pattern=[[-1, P]], channel_multiplier=1).then_inc(ident_ready, 1)
            pool.memset(minus_half[:], -0.5).then_inc(exponent_ready, 1)
            pool.wait_ge(exponent_ready, 1)

            def inverse_root(n, which):
                wait(pool, ln_var, n, 2, which + 1)
                pool.tensor_tensor(rstd[:], var_eps[:], minus_half[:], ALU.pow).then_inc(ln_rstd, 1)

            inverse_root(0, 0)
            inverse_root(0, 1)
            pool.wait_ge(bias_in, 16 * 4)

            def step(g, parity, more):
                wait(pool, xn1_ready, g, 2, 2)
                pool.tensor_tensor(xs[:, parity], xs[:, parity],
                                   bo[:].rearrange("p (a d) -> p a d", a=1).to_broadcast([P, PAIR, D]),
                                   ALU.add).then_inc(bo_added, 1)
                if more:
                    inverse_root(g + 1, 0)
                    inverse_root(g + 1, 1)

            over_pairs(pool, step)

        @block.scalar
        def _(act):
            act.dma_start(bq[:], bq1.rearrange("(c p) -> p c", p=P),
                          allow_slow_non_contiguous=True).then_inc(bias_in, 16)
            act.dma_start(bk[:], bk1.rearrange("(c p) -> p c", p=P),
                          allow_slow_non_contiguous=True).then_inc(bias_in, 16)
            act.dma_start(bv[:], bv1.rearrange("(c p) -> p c", p=P),
                          allow_slow_non_contiguous=True).then_inc(bias_in, 16)
            act.dma_start(bo[:], bo1.rearrange("(a d) -> a d", a=1).to_broadcast([P, D])).then_inc(bias_in, 16)
            for i in range(2 * C):
                act.wait_ge(wT_done, i + 1)
                nc.scalar.activation(wT[i // C][i % C], l0_bank[i % 2][:], ACT.Copy).then_inc(wT_ready, 1)

            def split_hi_weight(i):
                act.wait_ge(wraw_in[i], 16)
                nc.scalar.activation(split_into[i][0][:], stage[i % 2], ACT.Copy).then_inc(split_hi, 1)

            def m_row(r):
                act.wait_ge(m_done, r + 1)
                nc.scalar.activation(m_hi[:, r], l1_bank[r % 2][:], ACT.Copy).then_inc(m_hi_ready, 1)

            def relu_h0(n):
                for k in range(2):
                    wait(act, t0_done, n, 2, k + 1)
                    nc.scalar.activation(hT0[:, 2 * k:2 * k + 2].rearrange("p c b n -> p (c b n)"),
                                         l0_bank[k][:], ACT.Relu).then_inc(hT0_ready, 1)

            def copy_t(n, k):
                wait(act, t_done, n, 2, k + 1)
                nc.scalar.activation(tT[:, 2 * k:2 * k + 2].rearrange("p c b n -> p (c b n)"),
                                     l0_bank[k][:], ACT.Copy).then_inc(tT_ready, 1)

            def exp_alpha(n):
                wait(act, alpha_max, n, 1, 1)
                for b in range(PAIR):
                    last = nc.scalar.activation(alphaT[:, b], alphaT[:, b], ACT.Exp,
                                                bias=alpha_nmax[:, b:b + 1],
                                                accum_out=alpha_sum[:, b:b + 1])
                last.then_inc(alpha_exp, 1)

            def scale_hw(n, b):
                wait(act, alpha_ready, n, 1, 1)
                wait(act, hw_done, n, 2, b + 1)
                nc.scalar.activation(hw[:, b], l0_bank[b][:], ACT.Copy,
                                     scale=alpha_rsum[:, b:b + 1]).then_inc(hw_ready, 1)

            def relu_h1(n):
                for k in range(2):
                    wait(act, t1_done, n, 2, k + 1)
                    nc.scalar.activation(hT1_hi[:, 2 * k:2 * k + 2].rearrange("p c b n -> p (c b n)"),
                                         l0_bank[k][:], ACT.Relu).then_inc(hT1_hi_ready, 1)

            def copy_v(g, b):
                wait(act, v_done, g, 2, b + 1)
                nc.scalar.activation(v[:, b], l1_bank[b][:], ACT.Copy).then_inc(v_ready, 1)

            def place_q(g, c):
                wait(act, qk_done, g, 4, c + 1)
                wait(act, qk_split, g, 4, c)
                nc.scalar.activation(qT[:].rearrange("p b n -> p (b n)"), l1_bank[c % 2][:, 0:PAIR * P],
                                     ACT.Identity, bias=bq[:, c:c + 1])
                nc.scalar.activation(kT[:].rearrange("p b n -> p (b n)"), l1_bank[c % 2][:, PAIR * P:],
                                     ACT.Identity, bias=bk[:, c:c + 1]).then_inc(qk_ready, 1)

            def place_k(g, c):
                wait(act, qk_ready, g, 4, c + 1)
                for j in range(HC):
                    rows = slice(DH * j, DH * j + DH)
                    nc.scalar.activation(kbd_hi[rows, c % 2, :, j], kT[rows], ACT.Copy).then_inc(kbd_hi_ready, 1)

            def store(g, parity):
                wait(act, y_ready, g, 2, 2)
                act.wait_ge(x_in, 16)
                act.dma_start(out_pairs[g], xs[:, parity]).then_inc(stored, 16)

            def exp_scores(g, u):
                s = u % SLOTS
                wait(act, max_ready, g, UNITS, u + 1)
                for j in range(HC):
                    last = nc.scalar.activation(probs[:, s, j], probs[:, s, j], ACT.Exp,
                                                bias=nmax[:, s, j:j + 1], accum_out=sums[:, s, j:j + 1])
                last.then_inc(exp_ready, 1)

            def copy_probsT(g, u):
                wait(act, tr_done, g, UNITS, u + 1)
                nc.scalar.activation(probsT[:, u % SLOTS].rearrange("p h q -> p (h q)"), tr_bank[:],
                                     ACT.Copy).then_inc(probsT_ready, 1)

            def att_hi(g, c):
                wait(act, pv_done, g, C, c + 1)
                nc.scalar.activation(attT_hi[:, c].rearrange("p b n -> p (b n)"), pv_bank[:, 0:PAIR * P],
                                     ACT.Identity, bias=bv[:, c:c + 1]).then_inc(att_hi_ready, 1)

            split_hi_weight(2)
            split_hi_weight(3)
            m_row(0)
            m_row(1)
            relu_h0(0)
            split_hi_weight(4)
            m_row(2)
            m_row(3)
            split_hi_weight(5)
            split_hi_weight(6)
            copy_t(0, 0)
            copy_t(0, 1)
            exp_alpha(0)
            scale_hw(0, 0)
            scale_hw(0, 1)
            relu_h1(0)
            act.wait_ge(bias_in, 16 * 4)
            act.wait_ge(kbd_zero, 2)
            act.wait_ge(split_done, 5)

            def step(g, parity, more):
                n = g + 1
                place_q(g, 0)
                place_k(g, 0)
                place_q(g, 1)
                place_k(g, 1)
                if not isinstance(g, int) or g > 0:
                    store(g - 1, 1 - parity)
                exp_scores(g, 0)
                if more:
                    relu_h0(n)
                exp_scores(g, 1)
                copy_v(g, 0)
                copy_probsT(g, 0)
                copy_v(g, 1)
                copy_probsT(g, 1)
                exp_scores(g, 2)
                att_hi(g, 0)
                exp_scores(g, 3)
                place_q(g, 2)
                place_k(g, 2)
                copy_probsT(g, 2)
                if more:
                    copy_t(n, 0)
                copy_probsT(g, 3)
                att_hi(g, 1)
                exp_scores(g, 4)
                exp_scores(g, 5)
                if more:
                    copy_t(n, 1)
                place_q(g, 3)
                copy_probsT(g, 4)
                place_k(g, 3)
                copy_probsT(g, 5)
                if more:
                    exp_alpha(n)
                exp_scores(g, 6)
                if more:
                    scale_hw(n, 0)
                exp_scores(g, 7)
                att_hi(g, 2)
                if more:
                    scale_hw(n, 1)
                copy_probsT(g, 6)
                copy_probsT(g, 7)
                att_hi(g, 3)
                if more:
                    relu_h1(n)

            over_pairs(act, step)
            store(pairs - 1, 1)

        @block.vector
        def _(dve):
            def graph_stats(which, n, rows, b):
                if which == 1:
                    wait(dve, x1_ready, n, 2, b + 1)
                nc.vector.bn_stats(stats[:, b], rows[:, b]).then_inc(ln_stats, 1)

            def mean_var_eps(which, n):
                wait(dve, ln_stats, n, 4, 2 * which + 2)
                dve.sem_inc(stats_seen, 1)
                for b in range(PAIR):
                    nc.vector.bn_aggr(mean_var[:, b], stats[:, b]).then_inc(ln_aggr, 1)
                wait(dve, ln_aggr, n, 4, 2 * which + 2)
                nc.vector.tensor_scalar(var_eps[:].rearrange("p (b a) -> p b a", a=1), mean_var[:, :, 1:2], EPS,
                                        None, ALU.add).then_inc(ln_var, 1)

            def norm_apply(which, n, rows, xn):
                wait(dve, ln_rstd, n, 2, which + 1)
                for b in range(PAIR):
                    nc.vector.tensor_scalar(xn[:, b], rows[:, b], mean_var[:, b, 0:1], rstd[:, b:b + 1],
                                            ALU.subtract, ALU.mult).then_inc([xn0_ready, xn1_ready][which], 1)

            def norm0_stats(n):
                wait(dve, x_in, n, 16, 16)
                graph_stats(0, n, x_in_sb, 0)
                graph_stats(0, n, x_in_sb, 1)
                mean_var_eps(0, n)

            def masks(n, parity):
                wait(dve, adj_in, n, 16, 16)
                nc.vector.tensor_scalar(edge[:], adj_sb[:], 0.0, None, ALU.not_equal).then_inc(edge_ready, 1)
                wait(dve, edge_ready, n, 1, 1)
                nc.vector.tensor_reduce(has_edge[:], edge[:], AXIS.X, ALU.max).then_inc(edge_any, 1)
                wait(dve, edge_any, n, 1, 1)
                nc.vector.reciprocal(has_edge_r[:], has_edge[:]).then_inc(edge_rec, 1)
                wait(dve, edge_rec, n, 1, 1)
                nc.vector.scalar_tensor_tensor(low[:], has_edge_r[:], -BIG, has_edge[:], ALU.mult,
                                               ALU.mult).then_inc(low_ready, 1)
                wait(dve, low_ready, n, 1, 1)
                for b in range(PAIR):
                    last = nc.vector.tensor_scalar(mask_add[:, parity, b], adj_sb[:, b], 0.0, low[:, b:b + 1],
                                                   ALU.is_equal, ALU.mult)
                last.then_inc(mask_ready, 1)

            def split_q(g, c):
                wait(dve, qk_ready, g, 4, c + 1)
                nc.vector.tensor_copy(qT_hi[:, c % 2], qT[:]).then_inc(q_hi_ready, 1)
                wait(dve, q_hi_ready, g, 4, c + 1)
                nc.vector.tensor_tensor(qT_lo[:, c % 2], qT[:], qT_hi[:, c % 2].bitcast(F32), ALU.subtract)

            def split_k(g, c):
                for j in range(HC):
                    rows = slice(DH * j, DH * j + DH)
                    wait(dve, kbd_hi_ready, g, 4 * HC, c * HC + j + 1)
                    last = nc.vector.tensor_tensor(kbd_lo[rows, c % 2, :, j], kT[rows],
                                                   kbd_hi[rows, c % 2, :, j].bitcast(F32), ALU.subtract)
                last.then_inc(qk_split, 1)

            def split_h0(n):
                wait(dve, hT0_ready, n, 2, 2)
                nc.vector.tensor_copy(hT0_hi[:], hT0[:]).then_inc(hT0_hi_ready, 1)
                wait(dve, hT0_hi_ready, n, 1, 1)
                nc.vector.tensor_tensor(hT0_lo[:], hT0[:], hT0_hi[:].bitcast(F32),
                                        ALU.subtract).then_inc(hT0_split, 1)

            def mask_alpha(n):
                wait(dve, edgeT_done, n, 1, 1)
                nc.vector.tensor_copy(edgeT[:].rearrange("p b n -> p (b n)"),
                                      l0_bank[1][:, 0:PAIR * P]).then_inc(edgeT_ready, 1)
                wait(dve, edgeT_ready, n, 1, 1)
                wait(dve, alpha_done, n, 1, 1)
                nc.vector.scalar_tensor_tensor(alphaT[:].rearrange("p b n -> p (b n)"),
                                               l0_bank[0][:, 0:PAIR * P], 0.0,
                                               edgeT[:].rearrange("p b n -> p (b n)"),
                                               ALU.max, ALU.mult).then_inc(alpha_masked, 1)
                wait(dve, alpha_masked, n, 1, 1)
                nc.vector.tensor_reduce(alpha_nmax[:], alphaT[:], AXIS.X, ALU.max,
                                        negate=True).then_inc(alpha_max, 1)

            def alpha_sums(n):
                wait(dve, alpha_exp, n, 1, 1)
                nc.vector.reciprocal(alpha_rsum[:], alpha_sum[:]).then_inc(alpha_ready, 1)

            def residual0(n, parity, b):
                wait(dve, ao_done, n, 2, b + 1)
                wait(dve, stored, n, 16, -16)
                nc.vector.tensor_tensor(xs[:, parity, b], x_in_sb[:, b], l0_bank[b][:],
                                        ALU.add).then_inc(x1_ready, 1)

            def lo_h1(n, k):
                wait(dve, hT1_hi_ready, n, 2, k + 1)
                nc.vector.scalar_tensor_tensor(
                    hT1_lo[:, 2 * k:2 * k + 2].rearrange("p c b n -> p (c b n)"), l0_bank[k][:], 0.0,
                    hT1_hi[:, 2 * k:2 * k + 2].rearrange("p c b n -> p (c b n)").bitcast(F32),
                    ALU.max, ALU.subtract).then_inc(hT1_split, 1)

            def mask_scores(g, parity, u):
                s, b = u % SLOTS, u % PAIR
                wait(dve, score_done, g, UNITS, u + 1)
                wait(dve, tr_done, g, UNITS, u + 1 - SLOTS)
                mask_b = mask_add[:, parity, b:b + 1].to_broadcast([P, HC, P])
                nc.vector.scalar_tensor_tensor(probs[:, s], score_bank[u % 2][:].rearrange("p (h k) -> p h k", h=HC),
                                               SCALE, mask_b, ALU.mult, ALU.add).then_inc(score_masked, 1)
                wait(dve, score_masked, g, UNITS, u + 1)
                nc.vector.tensor_reduce(nmax[:, s], probs[:, s], AXIS.X, ALU.max,
                                        negate=True).then_inc(max_ready, 1)

            def normalise(g, u):
                s = u % SLOTS
                wait(dve, exp_ready, g, UNITS, u + 1)
                nc.vector.reciprocal(rsums[:, s], sums[:, s]).then_inc(rsum_ready, 1)
                wait(dve, rsum_ready, g, UNITS, u + 1)
                nc.vector.tensor_tensor(probs[:, s], probs[:, s],
                                        rsums[:, s].rearrange("p (h a) -> p h a", a=1).to_broadcast([P, HC, P]),
                                        ALU.mult).then_inc(probs_ready, 1)

            def att_lo(g, c):
                wait(dve, att_hi_ready, g, C, c + 1)
                nc.vector.scalar_tensor_tensor(attT_lo[:, c].rearrange("p b n -> p (b n)"),
                                               pv_bank[:, 0:PAIR * P], bv[:, c:c + 1],
                                               attT_hi[:, c].rearrange("p b n -> p (b n)").bitcast(F32),
                                               ALU.add, ALU.subtract).then_inc(att_split, 1)

            def residual1(g, parity, b):
                wait(dve, bo_added, g, 1, 1)
                wait(dve, o_done, g, 2, b + 1)
                nc.vector.tensor_tensor(xs[:, parity, b], xs[:, parity, b], l1_bank[b][:],
                                        ALU.add).then_inc(y_ready, 1)

            def split_lo_weight(i):
                hi, lo = split_into[i]
                dve.wait_ge(split_hi, i - 1)
                nc.vector.tensor_tensor(lo[:], stage[i % 2], hi[:].bitcast(F32),
                                        ALU.subtract).then_inc(split_done, 1)

            def m_row(r):
                dve.wait_ge(m_hi_ready, r + 1)
                nc.vector.tensor_tensor(m_lo[:, r], l1_bank[r % 2][:], m_hi[:, r].bitcast(F32),
                                        ALU.subtract).then_inc(m_ready, 1)

            norm0_stats(0)
            masks(0, 0)
            norm_apply(0, 0, x_in_sb, xn0)
            split_lo_weight(2)
            split_lo_weight(3)
            m_row(0)
            m_row(1)
            split_h0(0)
            split_lo_weight(4)
            m_row(2)
            m_row(3)
            split_lo_weight(5)
            split_lo_weight(6)
            mask_alpha(0)
            alpha_sums(0)
            residual0(0, 0, 0)
            graph_stats(1, 0, xs[:, 0], 0)
            residual0(0, 0, 1)
            graph_stats(1, 0, xs[:, 0], 1)
            mean_var_eps(1, 0)
            norm_apply(1, 0, xs[:, 0], xn1)
            lo_h1(0, 0)
            lo_h1(0, 1)
            dve.wait_ge(bias_in, 16 * 4)
            dve.wait_ge(kbd_zero, 2)

            def step(g, parity, more):
                n = g + 1
                if more:
                    norm0_stats(n)
                split_q(g, 0)
                split_k(g, 0)
                if more:
                    norm_apply(0, n, x_in_sb, xn0)
                split_q(g, 1)
                mask_scores(g, parity, 0)
                mask_scores(g, parity, 1)
                split_k(g, 1)
                normalise(g, 0)
                normalise(g, 1)
                mask_scores(g, parity, 2)
                if more:
                    split_h0(n)
                mask_scores(g, parity, 3)
                att_lo(g, 0)
                normalise(g, 2)
                normalise(g, 3)
                split_q(g, 2)
                split_k(g, 2)
                if more:
                    masks(n, 1 - parity)
                mask_scores(g, parity, 4)
                mask_scores(g, parity, 5)
                att_lo(g, 1)
                normalise(g, 4)
                normalise(g, 5)
                split_q(g, 3)
                split_k(g, 3)
                if more:
                    mask_alpha(n)
                mask_scores(g, parity, 6)
                if more:
                    alpha_sums(n)
                mask_scores(g, parity, 7)
                normalise(g, 6)
                normalise(g, 7)
                att_lo(g, 2)
                if more:
                    residual0(n, 1 - parity, 0)
                    graph_stats(1, n, xs[:, 1 - parity], 0)
                    residual0(n, 1 - parity, 1)
                    graph_stats(1, n, xs[:, 1 - parity], 1)
                    mean_var_eps(1, n)
                    norm_apply(1, n, xs[:, 1 - parity], xn1)
                att_lo(g, 3)
                if more:
                    lo_h1(n, 0)
                residual1(g, parity, 0)
                if more:
                    lo_h1(n, 1)
                residual1(g, parity, 1)

            over_pairs(dve, step)

        @block.tensor
        def _(pe):
            def by_rows(bank_out, hi, lo, b, weight_hi, weight_lo, first=0, end=C):
                for c in range(first, end):
                    nc.tensor.matmul(bank_out[:], hi[:, c, b], weight_hi[:, c], start=(c == 0), stop=False)
                    nc.tensor.matmul(bank_out[:], hi[:, c, b], weight_lo[:, c], start=False, stop=False)
                    last = nc.tensor.matmul(bank_out[:], lo[:, c, b], weight_hi[:, c], start=False,
                                            stop=(c == C - 1))
                return last

            def by_columns(region, weight_hi, weight_lo, cols, hi, lo, before=None):
                for c in range(C):
                    if before is not None:
                        before(c)
                    h_hi = hi[:, c].rearrange("p b n -> p (b n)")
                    h_lo = lo[:, c].rearrange("p b n -> p (b n)")
                    nc.tensor.matmul(region, weight_hi[:, c, cols], h_hi, start=(c == 0), stop=False)
                    nc.tensor.matmul(region, weight_hi[:, c, cols], h_lo, start=False, stop=False)
                    last = nc.tensor.matmul(region, weight_lo[:, c, cols], h_hi, start=False,
                                            stop=(c == C - 1))
                return last

            def chunk(c):
                return slice(c * P, c * P + P)

            def transpose_x(xn, done, b):
                for k in range(2):
                    for i in range(2):
                        last = nc.tensor.transpose(l0_bank[k][:, chunk(i * PAIR + b)], xn[:, b, chunk(2 * k + i)],
                                                   ident[:])
                    if b == PAIR - 1:
                        last.then_inc(done, 1)

            def transpose_x0(n):
                wait(pe, hT1_split, n, 2, 0)
                for b in range(PAIR):
                    wait(pe, xn0_ready, n, 2, b + 1)
                    transpose_x(xn0, t0_done, b)

            def project_t(n, c):
                wait(pe, hT0_split, n, 1, 1)
                half = c % 2
                last = by_columns(l0_bank[c // 2][:, half * PAIR * P:(half + 1) * PAIR * P], m_hi, m_lo,
                                  chunk(c), hT0_hi, hT0_lo)
                if half == 1:
                    last.then_inc(t_done, 1)

            def alpha_product(n):
                wait(pe, tT_ready, n, 2, 2)
                for b in range(PAIR):
                    for c in range(C):
                        last = nc.tensor.matmul(l0_bank[0][:, chunk(b)], hT0[:, c, b], tT[:, c, b],
                                                start=(c == 0), stop=(c == C - 1))
                last.then_inc(alpha_done, 1)
                wait(pe, mask_ready, n, 1, 1)
                for b in range(PAIR):
                    last = nc.tensor.transpose(l0_bank[1][:, chunk(b)], edge[:, b], ident[:])
                last.then_inc(edgeT_done, 1)

            def project_hw(n, b):
                wait(pe, alpha_masked, n, 1, 1)
                by_rows(l0_bank[b], hT0_hi, hT0_lo, b, w_hi, w_lo).then_inc(hw_done, 1)

            def alpha_hw(n, b):
                wait(pe, hw_ready, n, 2, b + 1)
                nc.tensor.matmul(l0_bank[b][:], alphaT[:, b], hw[:, b], start=True, stop=True).then_inc(ao_done, 1)

            def transpose_x1(n, b):
                wait(pe, xn1_ready, n, 2, b + 1)
                transpose_x(xn1, t1_done, b)

            def project_qk(g, c):
                def input_split(i):
                    if c == 0 and i % 2 == 0:
                        wait(pe, hT1_split, g, 2, i // 2 + 1)

                if c < 2:
                    wait(pe, y_ready, g, 2, c - 1)
                else:
                    wait(pe, v_ready, g, 2, c - 1)
                region = l1_bank[c % 2]
                by_columns(region[:, 0:PAIR * P], q_hi, q_lo, chunk(c), hT1_hi, hT1_lo, input_split)
                by_columns(region[:, PAIR * P:], k_hi, k_lo, chunk(c), hT1_hi, hT1_lo).then_inc(qk_done, 1)

            def project_v(g, b, first, end):
                if first == 0:
                    wait(pe, qk_ready, g, 4, b + 1)
                last = by_rows(l1_bank[b], hT1_hi, hT1_lo, b, v_hi, v_lo, first, end)
                if end == C:
                    last.then_inc(v_done, 1)

            def scores(g, u):
                c, b = u // PAIR, u % PAIR
                wait(pe, qk_split, g, 4, c + 1)
                wait(pe, score_masked, g, UNITS, u - 1)
                keys_hi = kbd_hi[:, c % 2, b].rearrange("p h k -> p (h k)")
                keys_lo = kbd_lo[:, c % 2, b].rearrange("p h k -> p (h k)")
                region = score_bank[u % 2][:]
                nc.tensor.matmul(region, qT_hi[:, c % 2, b], keys_hi, start=True, stop=False)
                nc.tensor.matmul(region, qT_hi[:, c % 2, b], keys_lo, start=False, stop=False)
                nc.tensor.matmul(region, qT_lo[:, c % 2, b], keys_hi, start=False,
                                 stop=True).then_inc(score_done, 1)

            def transpose_probs(g, u):
                wait(pe, probs_ready, g, UNITS, u + 1)
                wait(pe, probsT_ready, g, UNITS, u)
                for j in range(HC):
                    last = nc.tensor.transpose(tr_bank[:, chunk(j)], probs[:, u % SLOTS, j], ident[:])
                last.then_inc(tr_done, 1)

            def probs_v(g, u):
                c, b = u // PAIR, u % PAIR
                wait(pe, probsT_ready, g, UNITS, u + 1)
                wait(pe, v_ready, g, 2, b + 1)
                if b == 0:
                    wait(pe, att_split, g, C, c)
                for j in range(HC):
                    head = c * HC + j
                    last = nc.tensor.matmul(pv_bank[DH * j:DH * (j + 1), chunk(b)],
                                            v[:, b, head * DH:(head + 1) * DH], probsT[:, u % SLOTS, j],
                                            start=True, stop=True)
                if b == PAIR - 1:
                    last.then_inc(pv_done, 1)

            def project_o(g, b, first, end):
                wait(pe, att_split, g, C, end)
                if first == 0:
                    wait(pe, qk_ready, g, 4, 3 + b)
                last = by_rows(l1_bank[b], attT_hi, attT_lo, b, o_hi, o_lo, first, end)
                if end == C:
                    last.then_inc(o_done, 1)

            pe.wait_ge(ident_ready, 1)
            for i in range(2 * C):
                if i % C == 0:
                    pe.wait_ge(wraw_in[i // C], 16)
                if i >= 2:
                    pe.wait_ge(wT_ready, i - 1)
                for c in range(C):
                    last = nc.tensor.transpose(l0_bank[i % 2][:, chunk(c)], stage[i // C][:, c, chunk(i % C)], ident[:])
                last.then_inc(wT_done, 1)
            pe.wait_ge(wT_ready, 2 * C)
            for r in range(C):
                if r == 2:
                    transpose_x0(0)
                if r >= 2:
                    pe.wait_ge(m_ready, r - 1)
                for c in range(C):
                    last = nc.tensor.matmul(l1_bank[r % 2][:], wT[0][c][:, chunk(r)], wT[1][c],
                                            start=(c == 0), stop=(c == C - 1))
                last.then_inc(m_done, 1)
            pe.wait_ge(m_ready, C)
            for c in range(C):
                project_t(0, c)
            alpha_product(0)
            pe.wait_ge(split_done, 1)
            project_hw(0, 0)
            project_hw(0, 1)
            alpha_hw(0, 0)
            alpha_hw(0, 1)
            transpose_x1(0, 0)
            transpose_x1(0, 1)
            pe.wait_ge(split_done, 5)

            def step(g, parity, more):
                n = g + 1
                project_qk(g, 0)
                project_qk(g, 1)
                project_v(g, 0, 0, 2)
                scores(g, 0)
                scores(g, 1)
                if more:
                    transpose_x0(n)
                project_v(g, 0, 2, C)
                project_v(g, 1, 0, C)
                transpose_probs(g, 0)
                scores(g, 2)
                scores(g, 3)
                probs_v(g, 0)
                transpose_probs(g, 1)
                project_qk(g, 2)
                probs_v(g, 1)
                if more:
                    project_t(n, 0)
                    project_t(n, 1)
                transpose_probs(g, 2)
                if more:
                    project_t(n, 2)
                project_o(g, 0, 0, 1)
                probs_v(g, 2)
                transpose_probs(g, 3)
                scores(g, 4)
                scores(g, 5)
                probs_v(g, 3)
                if more:
                    project_t(n, 3)
                project_qk(g, 3)
                transpose_probs(g, 4)
                if more:
                    alpha_product(n)
                probs_v(g, 4)
                transpose_probs(g, 5)
                scores(g, 6)
                scores(g, 7)
                probs_v(g, 5)
                if more:
                    project_hw(n, 0)
                    project_hw(n, 1)
                    alpha_hw(n, 0)
                transpose_probs(g, 6)
                if more:
                    alpha_hw(n, 1)
                probs_v(g, 6)
                transpose_probs(g, 7)
                project_o(g, 0, 1, C - 1)
                probs_v(g, 7)
                project_o(g, 1, 0, C - 2)
                if more:
                    transpose_x1(n, 0)
                    transpose_x1(n, 1)
                project_o(g, 0, C - 1, C)
                project_o(g, 1, C - 2, C)

            over_pairs(pe, step)


_INS = ["x", "adj", "L0_gnn_weight", "L0_gnn_wq", "L0_gnn_wk", "L1_gnn_Wq", "L1_gnn_bq", "L1_gnn_Wk",
        "L1_gnn_bk", "L1_gnn_Wv", "L1_gnn_bv", "L1_gnn_Wo", "L1_gnn_bo"]


def kernel(**inputs):
    import numpy as np
    import concourse.bacc as bacc
    from concourse.bass_utils import run_bass_kernel_spmd

    nc = bacc.Bacc("TRN2", target_bir_lowering=False, num_devices=1)
    arrays, args = {}, []
    for name in _INS:
        a = np.ascontiguousarray(inputs[name])
        arrays[f"in_{name}"] = a
        args.append(nc.dram_tensor(f"in_{name}", a.shape, mybir.dt.from_np(a.dtype), kind="ExternalInput").ap())
    out = nc.dram_tensor("out_x", arrays["in_x"].shape, F32, kind="ExternalOutput").ap()
    graph_layers_kernel(nc, *args, out)
    result = run_bass_kernel_spmd(nc, [arrays], core_ids=[0])
    return result.results[0]["out_x"]
```
